# Optimizing a Trainium2 kernel written in Bass

```python
import numpy as np
import jax
import jax.numpy as jnp

def _softmax(x, axis=-1):
    return jax.nn.softmax(x, axis=axis)

def _gelu(x):
    return jax.nn.gelu(x, approximate=True)

def _silu(x):
    return jax.nn.silu(x)

def _sigmoid(x):
    return jax.nn.sigmoid(x)

def _layernorm(x, axis=-1, eps=1e-05):
    m = jnp.mean(x, axis=axis, keepdims=True)
    v = jnp.var(x, axis=axis, keepdims=True)
    return (x - m) / jnp.sqrt(v + eps)

def _scatter_add(tgt, idx, src, axis=0):
    return tgt.at[idx].add(src)

def _segment_sum(src, seg, n):
    return jax.ops.segment_sum(src, seg, n)
kernel_name = 'mk_macaron_d2_jaxref_r8_04b47e'

def setup_inputs(seed: int=0):
    np.random.seed(seed)
    _w = jnp.asarray

    def _L0_attn_setup():
        import jax, jax.numpy as jnp
        import numpy as np
        D_MODEL, D_STATE, D_CONV, D_INNER = (128, 16, 4, 256)
        BATCH, SEQLEN = (4, 256)

        def _mamba_fwd(x, W_in, conv_w, W_x, W_dt, b_dt, W_Bp, D_param, W_out):
            B, L, _ = x.shape
            xz = x @ W_in
            xc, z = jnp.split(xz, 2, axis=-1)
            xt = jnp.transpose(xc, (0, 2, 1))
            xt = jax.lax.conv_general_dilated(xt, conv_w, window_strides=(1,), padding=[(D_CONV - 1, 0)], dimension_numbers=('NCH', 'OIH', 'NCH'), feature_group_count=D_INNER)
            u = jax.nn.silu(jnp.transpose(xt, (0, 2, 1)))
            xp = u @ W_x
            dt_raw, B_raw = jnp.split(xp, 2, axis=-1)
            dt = jax.nn.softplus(dt_raw @ W_dt + b_dt)
            Bp = B_raw @ W_Bp
            dt = jnp.clip(dt, 0.0001, 1.0)
            ub = u * Bp

            def step(h, inp):
                d_t, ub_t = inp
                h = h * (1.0 - d_t) + ub_t
                return (h, h)
            _, ys = jax.lax.scan(step, jnp.zeros((B, D_INNER), x.dtype), (jnp.transpose(dt, (1, 0, 2)), jnp.transpose(ub, (1, 0, 2))))
            y = jnp.transpose(ys, (1, 0, 2)) + D_param * u
            y = y * jax.nn.silu(z)
            return y @ W_out
        key = jax.random.key(seed)
        ks = jax.random.split(key, 8)
        x = jax.random.normal(ks[0], (BATCH, SEQLEN, D_MODEL), jnp.float32)
        W_in = jax.random.normal(ks[1], (D_MODEL, 2 * D_INNER), jnp.float32) / np.float32(np.sqrt(D_MODEL))
        conv_w = jax.random.normal(ks[2], (D_INNER, 1, D_CONV), jnp.float32) * np.float32(0.3)
        W_x = jax.random.normal(ks[3], (D_INNER, 2 * D_STATE), jnp.float32) / np.float32(np.sqrt(D_INNER))
        W_dt = jax.random.normal(ks[4], (D_STATE, D_INNER), jnp.float32) / np.float32(np.sqrt(D_STATE))
        b_dt = jax.random.normal(ks[5], (D_INNER,), jnp.float32) * np.float32(0.1)
        W_Bp = jax.random.normal(ks[6], (D_STATE, D_INNER), jnp.float32) / np.float32(np.sqrt(D_STATE))
        D_param = jnp.ones((D_INNER,), jnp.float32)
        W_out = jax.random.normal(ks[7], (D_INNER, D_MODEL), jnp.float32) / np.float32(np.sqrt(D_INNER))
        return {'x': x, 'W_in': W_in, 'conv_w': conv_w, 'W_x': W_x, 'W_dt': W_dt, 'b_dt': b_dt, 'W_Bp': W_Bp, 'D_param': D_param, 'W_out': W_out}
    _L0_attn_in = _L0_attn_setup()

    def _L0_ffn_setup():
        import jax, jax.numpy as jnp
        import numpy as np
        E = 8
        K = 2
        key = jax.random.key(seed)
        ks = jax.random.split(key, 6)
        B, S, D, F = (4, 256, 128, 512)
        s_d = 1.0 / np.sqrt(D).astype(np.float32)
        s_f = 1.0 / np.sqrt(F).astype(np.float32)
        return {'x': jax.random.normal(ks[0], (B, S, D), jnp.float32), 'ln_w': jnp.ones((D,), jnp.float32), 'Wg': jax.random.normal(ks[1], (D, E), jnp.float32) * s_d, 'bg': jnp.zeros((E,), jnp.float32), 'W1a': jax.random.normal(ks[2], (E, D, F), jnp.float32) * s_d, 'b1a': jnp.zeros((E, F), jnp.float32), 'W1b': jax.random.normal(ks[3], (E, D, F), jnp.float32) * s_d, 'b1b': jnp.zeros((E, F), jnp.float32), 'W2': jax.random.normal(ks[4], (E, F, D), jnp.float32) * s_f, 'b2': jnp.zeros((E, D), jnp.float32)}
    _L0_ffn_in = _L0_ffn_setup()

    def _L1_attn_setup():
        import jax, jax.numpy as jnp
        import numpy as np
        from jax import lax
        D_MODEL = 128
        N_HEADS = 4
        D_STATE = 64
        D_CONV = 4
        EXPAND = 2
        D_INNER = EXPAND * D_MODEL
        DT_RANK = 64
        H_DIN = D_INNER // N_HEADS
        H_DT = DT_RANK // N_HEADS
        H_DS = D_STATE // N_HEADS
        BATCH, SEQ = (2, 128)
        key = jax.random.key(seed)
        ks = jax.random.split(key, 8)
        hidden_states = jax.random.normal(ks[0], (BATCH, SEQ, D_MODEL), dtype=jnp.float32)
        s_in = 1.0 / np.sqrt(D_MODEL)
        in_proj_w = jax.random.uniform(ks[1], (2 * D_INNER, D_MODEL), minval=-s_in, maxval=s_in)
        s_c = 1.0 / np.sqrt(D_CONV)
        conv_w = jax.random.uniform(ks[2], (D_INNER, 1, D_CONV), minval=-s_c, maxval=s_c)
        conv_b = jax.random.uniform(ks[3], (D_INNER,), minval=-s_c, maxval=s_c)
        s_x = 1.0 / np.sqrt(H_DIN)
        x_proj_w = jax.random.uniform(ks[4], ((2 * H_DS + H_DT) * N_HEADS, H_DIN), minval=-s_x, maxval=s_x)
        s_dt = H_DT ** (-0.5)
        dt_proj_w = jax.random.uniform(ks[5], (D_INNER, H_DT), minval=-s_dt, maxval=s_dt)
        dt = jnp.exp(jax.random.uniform(ks[6], (D_INNER,)) * (np.log(0.1) - np.log(0.001)) + np.log(0.001))
        dt = jnp.clip(dt, 0.0001, None)
        dt_proj_b = dt + jnp.log(-jnp.expm1(-dt))
        A_log = jnp.log(jnp.tile(jnp.arange(1, H_DS + 1, dtype=jnp.float32), (D_INNER, 1)))
        Dskip = jnp.ones((D_INNER,), dtype=jnp.float32)
        out_proj_w = jax.random.uniform(ks[7], (D_MODEL, D_INNER), minval=-s_x, maxval=s_x)
        return {'hidden_states': hidden_states, 'in_proj_w': in_proj_w, 'conv_w': conv_w, 'conv_b': conv_b, 'x_proj_w': x_proj_w, 'dt_proj_w': dt_proj_w, 'dt_proj_b': dt_proj_b, 'A_log': A_log, 'Dskip': Dskip, 'out_proj_w': out_proj_w}
    _L1_attn_in = _L1_attn_setup()

    def _L1_ffn_setup():
        import jax, jax.numpy as jnp
        import numpy as np
        NUM_EXPERTS = 8
        TOP_K = 2
        CAP_RATIO = 1.25
        INIT_STD = 0.02
        key = jax.random.key(seed)
        k1, k2, k3, k4 = jax.random.split(key, 4)
        B, T, H, F = (4, 256, 128, 512)
        x = jax.random.normal(k1, (B, T, H), jnp.float32)
        router_w = jax.random.normal(k2, (NUM_EXPERTS, H), jnp.float32) * INIT_STD
        w1 = jax.random.normal(k3, (NUM_EXPERTS, H, F), jnp.float32) * INIT_STD
        w2 = jax.random.normal(k4, (NUM_EXPERTS, F, H), jnp.float32) * INIT_STD
        return {'x': x, 'router_w': router_w, 'w1': w1, 'w2': w2}
    _L1_ffn_in = _L1_ffn_setup()
    _d = {'L0_attn_x': _L0_attn_in['x'], 'L0_attn_W_in': _L0_attn_in['W_in'], 'L0_attn_conv_w': _L0_attn_in['conv_w'], 'L0_attn_W_x': _L0_attn_in['W_x'], 'L0_attn_W_dt': _L0_attn_in['W_dt'], 'L0_attn_b_dt': _L0_attn_in['b_dt'], 'L0_attn_W_Bp': _L0_attn_in['W_Bp'], 'L0_attn_D_param': _L0_attn_in['D_param'], 'L0_attn_W_out': _L0_attn_in['W_out'], 'L0_ffn_ln_w': _L0_ffn_in['ln_w'], 'L0_ffn_Wg': _L0_ffn_in['Wg'], 'L0_ffn_bg': _L0_ffn_in['bg'], 'L0_ffn_W1a': _L0_ffn_in['W1a'], 'L0_ffn_b1a': _L0_ffn_in['b1a'], 'L0_ffn_W1b': _L0_ffn_in['W1b'], 'L0_ffn_b1b': _L0_ffn_in['b1b'], 'L0_ffn_W2': _L0_ffn_in['W2'], 'L0_ffn_b2': _L0_ffn_in['b2'], 'L1_attn_in_proj_w': _L1_attn_in['in_proj_w'], 'L1_attn_conv_w': _L1_attn_in['conv_w'], 'L1_attn_conv_b': _L1_attn_in['conv_b'], 'L1_attn_x_proj_w': _L1_attn_in['x_proj_w'], 'L1_attn_dt_proj_w': _L1_attn_in['dt_proj_w'], 'L1_attn_dt_proj_b': _L1_attn_in['dt_proj_b'], 'L1_attn_A_log': _L1_attn_in['A_log'], 'L1_attn_Dskip': _L1_attn_in['Dskip'], 'L1_attn_out_proj_w': _L1_attn_in['out_proj_w'], 'L1_ffn_router_w': _L1_ffn_in['router_w'], 'L1_ffn_w1': _L1_ffn_in['w1'], 'L1_ffn_w2': _L1_ffn_in['w2']}
    _x0 = _d['L0_attn_x']
    _d['L0_attn_x'] = jax.random.normal(jax.random.fold_in(jax.random.key(seed), 1), (8, 1024, 128), dtype=_x0.dtype)
    del _x0
    return _d

def reference(L0_attn_x, L0_attn_W_in, L0_attn_conv_w, L0_attn_W_x, L0_attn_W_dt, L0_attn_b_dt, L0_attn_W_Bp, L0_attn_D_param, L0_attn_W_out, L0_ffn_ln_w, L0_ffn_Wg, L0_ffn_bg, L0_ffn_W1a, L0_ffn_b1a, L0_ffn_W1b, L0_ffn_b1b, L0_ffn_W2, L0_ffn_b2, L1_attn_in_proj_w, L1_attn_conv_w, L1_attn_conv_b, L1_attn_x_proj_w, L1_attn_dt_proj_w, L1_attn_dt_proj_b, L1_attn_A_log, L1_attn_Dskip, L1_attn_out_proj_w, L1_ffn_router_w, L1_ffn_w1, L1_ffn_w2):

    def _L0_attn_ref(x, W_in, conv_w, W_x, W_dt, b_dt, W_Bp, D_param, W_out):
        import jax, jax.numpy as jnp
        import numpy as np
        D_MODEL, D_STATE, D_CONV, D_INNER = (128, 16, 4, 256)
        BATCH, SEQLEN = (4, 256)

        def _mamba_fwd(x, W_in, conv_w, W_x, W_dt, b_dt, W_Bp, D_param, W_out):
            B, L, _ = x.shape
            xz = x @ W_in
            xc, z = jnp.split(xz, 2, axis=-1)
            xt = jnp.transpose(xc, (0, 2, 1))
            xt = jax.lax.conv_general_dilated(xt, conv_w, window_strides=(1,), padding=[(D_CONV - 1, 0)], dimension_numbers=('NCH', 'OIH', 'NCH'), feature_group_count=D_INNER)
            u = jax.nn.silu(jnp.transpose(xt, (0, 2, 1)))
            xp = u @ W_x
            dt_raw, B_raw = jnp.split(xp, 2, axis=-1)
            dt = jax.nn.softplus(dt_raw @ W_dt + b_dt)
            Bp = B_raw @ W_Bp
            dt = jnp.clip(dt, 0.0001, 1.0)
            ub = u * Bp

            def step(h, inp):
                d_t, ub_t = inp
                h = h * (1.0 - d_t) + ub_t
                return (h, h)
            _, ys = jax.lax.scan(step, jnp.zeros((B, D_INNER), x.dtype), (jnp.transpose(dt, (1, 0, 2)), jnp.transpose(ub, (1, 0, 2))))
            y = jnp.transpose(ys, (1, 0, 2)) + D_param * u
            y = y * jax.nn.silu(z)
            return y @ W_out
        return _mamba_fwd(x, W_in, conv_w, W_x, W_dt, b_dt, W_Bp, D_param, W_out)

    def _L0_ffn_ref(x, ln_w, Wg, bg, W1a, b1a, W1b, b1b, W2, b2):
        import jax, jax.numpy as jnp
        import numpy as np
        E = 8
        K = 2
        B, S, D = x.shape
        eps = jnp.finfo(x.dtype).eps
        xn = x * jax.lax.rsqrt(jnp.mean(x * x, axis=-1, keepdims=True) + eps) * ln_w
        logits = xn @ Wg + bg
        vals, idx = jax.lax.top_k(logits, K)
        topk_w = jax.nn.softmax(vals, axis=-1)
        we = jnp.sum(jax.nn.one_hot(idx, E, dtype=x.dtype) * topk_w[..., None], axis=-2)
        T = B * S
        xf = xn.reshape(T, D)
        wef = we.reshape(T, E).T

        def step(acc, params):
            W1a_e, b1a_e, W1b_e, b1b_e, W2_e, b2_e, w_e = params
            a = xf @ W1a_e + b1a_e
            b = xf @ W1b_e + b1b_e
            y = jax.nn.silu(a) * b @ W2_e + b2_e
            return (acc + w_e[:, None] * y, None)
        out0 = jnp.zeros_like(xf)
        out, _ = jax.lax.scan(step, out0, (W1a, b1a, W1b, b1b, W2, b2, wef))
        return out.reshape(B, S, D)

    def _L1_attn_ref(hidden_states, in_proj_w, conv_w, conv_b, x_proj_w, dt_proj_w, dt_proj_b, A_log, Dskip, out_proj_w):
        import jax, jax.numpy as jnp
        import numpy as np
        from jax import lax
        D_MODEL = 128
        N_HEADS = 4
        D_STATE = 64
        D_CONV = 4
        EXPAND = 2
        D_INNER = EXPAND * D_MODEL
        DT_RANK = 64
        H_DIN = D_INNER // N_HEADS
        H_DT = DT_RANK // N_HEADS
        H_DS = D_STATE // N_HEADS
        BATCH, SEQ = (2, 128)
        b, L, _ = hidden_states.shape
        xz = hidden_states @ in_proj_w.T
        x, z = jnp.split(xz, 2, axis=-1)
        xp = jnp.pad(x, ((0, 0), (D_CONV - 1, 0), (0, 0)))
        w = conv_w[:, 0, :]
        xc = conv_b
        for k in range(D_CONV):
            xc = xc + xp[:, k:k + L, :] * w[:, k]
        x = jax.nn.silu(xc)
        xh = x.reshape(b, L, N_HEADS, H_DIN)
        xw = x_proj_w.reshape(N_HEADS, 2 * H_DS + H_DT, H_DIN)
        x_dbl = jnp.einsum('hod,blhd->blho', xw, xh)
        dt_r, Bm, Cm = jnp.split(x_dbl, [H_DT, H_DT + H_DS], axis=-1)
        dtw = dt_proj_w.reshape(N_HEADS, H_DIN, H_DT)
        delta = jnp.einsum('hdr,blhr->blhd', dtw, dt_r)
        delta = jax.nn.softplus(delta + dt_proj_b.reshape(N_HEADS, H_DIN))
        A = -jnp.exp(A_log).reshape(N_HEADS, H_DIN, H_DS)

        def step(s, inp):
            d_t, u_t, B_t, C_t = inp
            dA = jnp.exp(d_t[..., None] * A)
            s = s * dA + (d_t * u_t)[..., None] * B_t[:, :, None, :]
            y_t = jnp.einsum('bhdn,bhn->bhd', s, C_t)
            return (s, y_t)
        s0 = jnp.zeros((b, N_HEADS, H_DIN, H_DS), dtype=x.dtype)
        scan_in = (delta.transpose(1, 0, 2, 3), xh.transpose(1, 0, 2, 3), Bm.transpose(1, 0, 2, 3), Cm.transpose(1, 0, 2, 3))
        _, ys = lax.scan(step, s0, scan_in)
        y = ys.transpose(1, 0, 2, 3).reshape(b, L, D_INNER)
        y = y + x * Dskip
        y = y * jax.nn.silu(z)
        out = y @ out_proj_w.T
        return out

    def _L1_ffn_ref(x, router_w, w1, w2):
        import jax, jax.numpy as jnp
        import numpy as np
        NUM_EXPERTS = 8
        TOP_K = 2
        CAP_RATIO = 1.25
        INIT_STD = 0.02
        B, T, H = x.shape
        E, K = (NUM_EXPERTS, TOP_K)
        xf = x.reshape(-1, H)
        N = xf.shape[0]
        P = N * K
        capacity = int(CAP_RATio * N * K / E) + 1 if False else int(CAP_RATIO * N * K / E) + 1
        logits = xf @ router_w.T
        probs = jax.nn.softmax(logits, axis=-1)
        k_probs, k_idx = jax.lax.top_k(probs, K)
        k_probs = k_probs / jnp.sum(k_probs, axis=-1, keepdims=True)
        flat_e = k_idx.reshape(-1)
        onehot = jax.nn.one_hot(flat_e, E, dtype=jnp.int32)
        rank = jnp.take_along_axis(jnp.cumsum(onehot, axis=0) - 1, flat_e[:, None], axis=1)[:, 0]
        keep = rank < capacity
        slot = jnp.minimum(rank, capacity - 1)
        token_id = jnp.arange(P) // K
        dispatched = jnp.where(keep[:, None], xf[token_id], 0.0)
        buf = jnp.zeros((E, capacity, H), x.dtype).at[flat_e, slot].add(dispatched)
        h = jax.nn.silu(jnp.einsum('ech,ehf->ecf', buf, w1))
        out_buf = jnp.einsum('ecf,efh->ech', h, w2)
        pair_out = out_buf[flat_e, slot] * keep[:, None].astype(x.dtype)
        combined = jnp.sum(pair_out.reshape(N, K, H) * k_probs[..., None], axis=1)
        return combined.reshape(B, T, H) + x
    x = L0_attn_x
    x = x + 0.5 * _L0_ffn_ref(_layernorm(x, axis=-1), L0_ffn_ln_w, L0_ffn_Wg, L0_ffn_bg, L0_ffn_W1a, L0_ffn_b1a, L0_ffn_W1b, L0_ffn_b1b, L0_ffn_W2, L0_ffn_b2)
    x = x + _L0_attn_ref(_layernorm(x, axis=-1), L0_attn_W_in, L0_attn_conv_w, L0_attn_W_x, L0_attn_W_dt, L0_attn_b_dt, L0_attn_W_Bp, L0_attn_D_param, L0_attn_W_out)
    x = x + 0.5 * _L0_ffn_ref(_layernorm(x, axis=-1), L0_ffn_ln_w, L0_ffn_Wg, L0_ffn_bg, L0_ffn_W1a, L0_ffn_b1a, L0_ffn_W1b, L0_ffn_b1b, L0_ffn_W2, L0_ffn_b2)
    x = x + 0.5 * _L1_ffn_ref(_layernorm(x, axis=-1), L1_ffn_router_w, L1_ffn_w1, L1_ffn_w2)
    x = x + _L1_attn_ref(_layernorm(x, axis=-1), L1_attn_in_proj_w, L1_attn_conv_w, L1_attn_conv_b, L1_attn_x_proj_w, L1_attn_dt_proj_w, L1_attn_dt_proj_b, L1_attn_A_log, L1_attn_Dskip, L1_attn_out_proj_w)
    x = x + 0.5 * _L1_ffn_ref(_layernorm(x, axis=-1), L1_ffn_router_w, L1_ffn_w1, L1_ffn_w2)
    return x

_drawn_inputs = setup_inputs


def setup_inputs(seed=0):
    import zlib

    import numpy as np

    out = dict(_drawn_inputs(seed))
    spreads = {'L0_attn_D_param': (1.0, 0.2),
     'L0_ffn_ln_w': (1.0, 0.2),
     'L0_ffn_bg': (0.0, 0.1),
     'L0_ffn_b1a': (0.0, 0.1),
     'L0_ffn_b1b': (0.0, 0.1),
     'L0_ffn_b2': (0.0, 0.1),
     'L1_attn_Dskip': (1.0, 0.6)}
    factors = {'L0_attn_W_dt': 2.77,
     'L0_attn_b_dt': 6.009,
     'L1_attn_x_proj_w': 8.0,
     'L1_attn_dt_proj_w': 8.0,
     'L1_attn_dt_proj_b': 8.0,
     'L1_attn_A_log': 8.0,
     'L1_ffn_router_w': 3.252,
     'L1_ffn_w1': 2.858,
     'L1_ffn_w2': 2.849}
    for name, (base, spread) in spreads.items():
        noise = np.random.default_rng([zlib.crc32(name.encode()), seed]).standard_normal(out[name].shape)
        drawn = base * np.exp(spread * noise) if base else spread * noise
        out[name] = jnp.asarray(drawn.astype(out[name].dtype))
    for name, factor in factors.items():
        out[name] = (out[name] * factor).astype(out[name].dtype)
    return out
```

```python
import numpy as np
import concourse.bass as bass
from concourse import mybir
from contextlib import ExitStack, contextmanager

F32 = mybir.dt.float32
BF16 = mybir.dt.bfloat16
I32 = mybir.dt.int32
ALU = mybir.AluOpType
ACT = mybir.ActivationFunctionType
AX = mybir.AxisListType

P = 128
D = 128
SEQS = 8
SEQ = 1024
TOK = SEQS * SEQ
NT = TOK // P
E = 8
F = 512
FC = F // P
BLK = 256
NBLK = 2 * TOK // BLK + E
ROWS = NBLK * BLK
CAP = int(1.25 * TOK * 2 / E) + 1
LN_EPS = 1e-5
RMS_EPS = float(np.finfo(np.float32).eps)
GRP = 4
NG = NT // GRP
INNER = 256
HALVES = INNER // P
CONV = 4


def wait(eng, sem, value):
    if isinstance(value, int) and value <= 0:
        return
    eng.wait_ge(sem, value)


def two_slot_loop(eng, n, step):
    step(0, 0)
    step(1, 1)
    with eng.Fori(0, (n - 2) // 2) as i:
        step(i * 2 + 2, 0)
        step(i * 2 + 3, 1)


def at(t, size=1):
    return slice(t * size, (t + 1) * size) if isinstance(t, int) else bass.ds(t * size, size)


class Core:
    pass


def chain(eng, sem):
    count = [0]

    def link(ins):
        count[0] += 1
        ins.then_inc(sem, 1)
        eng.wait_ge(sem, count[0])
    return link


@contextmanager
def layer_semaphores(nc):
    before = nc.snapshot_sems()
    yield
    nc.all_engine_barrier()
    nc.clear_and_free_semaphores(nc.allocated_since(before))
    nc.all_engine_barrier()


def load_and_constants(nc, c, x_dram):
    with ExitStack() as ctx:
        x_loaded = nc.alloc_semaphore("x_loaded")
        zero_ready = nc.alloc_semaphore("zero_ready")
        rows_cleared = nc.alloc_semaphore("rows_cleared")
        pool_step = nc.alloc_semaphore("const_pool_step")
        dve_step = nc.alloc_semaphore("const_dve_step")
        zeros = ctx.enter_context(nc.sbuf_tensor("zeros", [P, 29 * D], F32))
        iota_i = ctx.enter_context(nc.sbuf_tensor("iota_i", [P, NT, E], I32))
        part_i = ctx.enter_context(nc.sbuf_tensor("part_i", [P, 1], I32))
        blk_i = ctx.enter_context(nc.sbuf_tensor("blk_i", [P, NBLK + 2], I32))
        block = ctx.enter_context(nc.Block())
        x_v = x_dram.rearrange("b s d -> (b s) d").rearrange("(j p) d -> p j d", p=P)
        rows_v = c.rows_in.rearrange("(p r) d -> p (r d)", p=P)
        nclear = (ROWS + P) // P // 29

        @block.sync
        def _(sp):
            for q in range(2):
                sp.dma_start(c.x[:, at(q, NT // 2), :], x_v[:, at(q, NT // 2), :]).then_inc(x_loaded, 16)
            sp.wait_ge(zero_ready, 1)
            for q in range(nclear):
                sp.dma_start(rows_v[:, at(q, 29 * D)], zeros[:, :]).then_inc(rows_cleared, 16)
            sp.wait_ge(x_loaded, 32)
            sp.wait_ge(rows_cleared, 16 * nclear)

        @block.gpsimd
        def _(pool):
            link = chain(pool, pool_step)
            nc.gpsimd.memset(zeros[:, :], 0.0).then_inc(zero_ready, 1)
            link(nc.gpsimd.memset(c.ident[:, :], 0.0))
            link(nc.gpsimd.affine_select(out=c.ident[:, :], in_=c.ident[:, :], compare_op=ALU.not_equal,
                                         fill=1.0, base=0, pattern=[[-1, P]], channel_multiplier=1))
            link(nc.gpsimd.memset(c.before[:, :], 1.0))
            link(nc.gpsimd.affine_select(out=c.before[:, :], in_=c.before[:, :], compare_op=ALU.is_gt,
                                         fill=0.0, base=0, pattern=[[1, P]], channel_multiplier=-1))
            link(nc.gpsimd.memset(c.ones_bf[:, :], 1.0))
            link(nc.gpsimd.memset(c.ones_f[:, :], 1.0))
            link(nc.gpsimd.memset(c.minus_half[:, :], -0.5))
            link(nc.gpsimd.iota(iota_i[:, :, :], pattern=[[0, NT], [1, E]], base=0, channel_multiplier=0))
            link(nc.gpsimd.iota(part_i[:, :], pattern=[[0, 1]], base=ROWS, channel_multiplier=1))
            link(nc.gpsimd.iota(blk_i[:, :], pattern=[[BLK, NBLK + 2]], base=0, channel_multiplier=0))

        @block.vector
        def _(dve):
            dve.wait_ge(pool_step, 10)
            nc.vector.tensor_copy(c.expert_id[:, :, :], iota_i[:, :, :])
            nc.vector.tensor_copy(c.drop_row[:, :], part_i[:, :])
            nc.vector.tensor_copy(c.block_row[:, :], blk_i[:, :])


def row_statistics(nc, c, tag, mean, rstd, rms):
    with ExitStack() as ctx:
        stats = ctx.enter_context(nc.sbuf_tensor(f"{tag}_stats", [P, NT, 6], F32))
        var = ctx.enter_context(nc.sbuf_tensor(f"{tag}_var", [P, NT], F32))
        dif = ctx.enter_context(nc.sbuf_tensor(f"{tag}_dif", [P, NT], F32))
        stat_step = nc.alloc_semaphore(f"{tag}_stat_step")
        dve_step = nc.alloc_semaphore(f"{tag}_var_step")
        pool_step = nc.alloc_semaphore(f"{tag}_rstd_step")
        var_ready = nc.alloc_semaphore(f"{tag}_var_ready")
        block = ctx.enter_context(nc.Block())

        @block.vector
        def _(dve):
            with dve.Fori(0, NG) as g:
                for k in range(GRP):
                    nc.vector.bn_stats(stats[:, at(g * GRP + k), :], c.x[:, at(g * GRP + k), :]).then_inc(stat_step, 1)
            dve.wait_ge(stat_step, NT)
            link = chain(dve, dve_step)
            link(nc.vector.tensor_tensor(dif[:, :], stats[:, :, 1], stats[:, :, 4], ALU.subtract))
            link(nc.vector.tensor_tensor(dif[:, :], dif[:, :], dif[:, :], ALU.mult))
            link(nc.vector.tensor_tensor(var[:, :], stats[:, :, 2], stats[:, :, 5], ALU.add))
            link(nc.vector.tensor_scalar(dif[:, :], dif[:, :], 0.25, None, ALU.mult))
            nc.vector.scalar_tensor_tensor(out=var[:, :], in0=var[:, :], scalar=1.0 / D, in1=dif[:, :],
                                           op0=ALU.mult, op1=ALU.add).then_inc(var_ready, 1)
            link(nc.vector.tensor_tensor(mean[:, :], stats[:, :, 1], stats[:, :, 4], ALU.add))
            nc.vector.tensor_scalar(mean[:, :], mean[:, :], 0.5, None, ALU.mult)

        @block.gpsimd
        def _(pool):
            link = chain(pool, pool_step)

            def rsqrt(dst, src, eps):
                link(nc.gpsimd.tensor_scalar(dst, src, eps, None, ALU.add))
                link(nc.gpsimd.tensor_tensor(dst, dst, c.minus_half[:, :], ALU.pow))
            pool.wait_ge(var_ready, 1)
            rsqrt(rstd[:, :], var[:, :], LN_EPS)
            if rms:
                link(nc.gpsimd.tensor_tensor(var[:, :], var[:, :], rstd[:, :], ALU.mult))
                link(nc.gpsimd.tensor_tensor(var[:, :], var[:, :], rstd[:, :], ALU.mult))
                rsqrt(var[:, :], var[:, :], RMS_EPS)
                link(nc.gpsimd.tensor_tensor(rstd[:, :], rstd[:, :], var[:, :], ALU.mult))


def moe(nc, c, tag, gated, w):
    PACK = 3 * F + 2 * FC + D if gated else 2 * F
    W1A, W1B, W2 = 0, F, (2 * F if gated else F)
    B1A, B1B, B2 = 3 * F, 3 * F + FC, 3 * F + 2 * FC
    with ExitStack() as ctx:
        def sb(name, shape, dt=F32):
            return ctx.enter_context(nc.sbuf_tensor(f"{tag}_{name}", shape, dt))

        def sem(name):
            return nc.alloc_semaphore(f"{tag}_{name}")

        packs = sb("packs", [P, E, PACK])
        gate_w = sb("gate_w", [D, E])
        rstd = sb("rstd", [P, NT])
        mean = sb("mean", [P, NT])
        weight = [sb(f"weight{k}", [P, NT]) for k in range(2)]
        put_i = [sb(f"put{k}", [P, NT], I32) for k in range(2)]
        get_i = [sb(f"get{k}", [P, NT], I32) for k in range(2)]
        block_pack = sb("block_pack", [P, NBLK + 2], I32)
        w_loaded = sem("w_loaded")
        gate_loaded = sem("gate_loaded")
        if gated:
            ln_w = sb("ln_w", [P, D])
            gate_b = sb("gate_b", [P, E])
        packs_3d = packs[:, :, :]

        row_statistics(nc, c, tag, mean, rstd, gated)

        with ExitStack() as rc:
            def rsb(name, shape, dt=F32):
                return rc.enter_context(nc.sbuf_tensor(f"{tag}_{name}", shape, dt))

            xc = rsb("xc", [P, 2, GRP, D])
            xcT = rsb("xcT", [D, 2, GRP * P])
            L = rsb("L", [P, NT, E])
            oh = [rsb(f"oh{k}", [P, NT, E]) for k in range(2)]
            t8 = rsb("t8", [P, NT, E])
            u8 = rsb("u8", [P, NT, E])
            chosen = rsb("chosen", [P, NT, E], BF16)
            m = [rsb(f"m{k}", [P, NT]) for k in range(2)]
            ind = rsb("ind", [P, NT])
            rank = rsb("rank", [P, NT])
            base_k = rsb("base_k", [P, NT])
            keep = rsb("keep", [P, NT])
            cum = rsb("cum", [P, E, NT])
            cnt = rsb("cnt", [P, E])
            cnt_i = rsb("cnt_i", [P, E], I32)
            run_end = rsb("run_end", [P, E])
            run_base = rsb("run_base", [P, E])
            bmap = rsb("bmap", [P, NBLK + 2])
            tps = [rc.enter_context(nc.psum_tensor(f"{tag}_tps{u}", [P, GRP * P], F32)) for u in range(2)]
            lps = rc.enter_context(nc.psum_tensor(f"{tag}_lps", [P, NT * E], F32))
            pre_ps = rc.enter_context(nc.psum_tensor(f"{tag}_pre", [P, NT * E], F32))
            tot_ps = rc.enter_context(nc.psum_tensor(f"{tag}_tot", [P, NT * E], F32))
            lps3 = lps[:, :].rearrange("p (t e) -> p t e", e=E)
            pre3 = pre_ps[:, :].rearrange("p (t e) -> p t e", e=E)
            tot3 = tot_ps[:, :].rearrange("p (t e) -> p t e", e=E)

            def rsem(name):
                return nc.alloc_semaphore(f"{tag}_{name}")
            dve_step = rsem("route_dve_step")
            centred = rsem("centred")
            transposed = rsem("transposed")
            copied = rsem("copied")
            logits_done = rsem("logits_done")
            logits_shifted = rsem("logits_shifted")
            exp_done = rsem("exp_done")
            chosen_ready = rsem("chosen_ready")
            counted = rsem("counted")
            block = rc.enter_context(nc.Block())

            @block.sync
            def _(sp):
                sp.dma_start(gate_w[:, :], w["gate"], allow_slow_non_contiguous=True).then_inc(gate_loaded, 16)
                if gated:
                    sp.dma_start(ln_w[:, :], w["ln_w"].rearrange("(a d) -> a d", a=1).to_broadcast([P, D])).then_inc(gate_loaded, 16)
                    sp.dma_start(gate_b[:, :], w["gate_b"].rearrange("(a d) -> a d", a=1).to_broadcast([P, E])).then_inc(gate_loaded, 16)
                for name, off, width in w["packed"]:
                    sp.dma_start(packs_3d[:, :, off:off + width], name).then_inc(w_loaded, 16)
                if gated:
                    for k in range(FC):
                        sp.dma_start(packs_3d[:, :, B1A + k], w["b1a"][:, at(k, P)].rearrange("e f -> f e"), allow_slow_non_contiguous=True).then_inc(w_loaded, 16)
                        sp.dma_start(packs_3d[:, :, B1B + k], w["b1b"][:, at(k, P)].rearrange("e f -> f e"), allow_slow_non_contiguous=True).then_inc(w_loaded, 16)
                    sp.dma_start(packs_3d[:, :, B2:B2 + D], w["b2"].rearrange("(a e) d -> a e d", a=1).to_broadcast([P, E, D])).then_inc(w_loaded, 16)

            @block.vector
            def _(dve):
                link = chain(dve, dve_step)
                dve.wait_ge(gate_loaded, 48 if gated else 16)

                def centre(g, slot):
                    wait(dve, transposed, g - 1)
                    for k in range(GRP):
                        t = g * GRP + k
                        if gated:
                            ins = nc.vector.scalar_tensor_tensor(
                                out=xc[:, slot, k:k + 1, :], in0=c.x[:, at(t), :], scalar=mean[:, at(t)],
                                in1=ln_w[:, :].unsqueeze(1), op0=ALU.subtract, op1=ALU.mult)
                        else:
                            ins = nc.vector.tensor_scalar(xc[:, slot, k:k + 1, :], c.x[:, at(t), :], mean[:, at(t)],
                                                          None, ALU.subtract)
                        ins.then_inc(centred, 1)
                two_slot_loop(dve, NG, centre)
                dve.wait_ge(logits_done, NG)
                rb = rstd[:, :].unsqueeze(2).to_broadcast([P, NT, E])
                link(nc.vector.tensor_tensor(L[:, :, :], lps3, rb, ALU.mult))
                if gated:
                    link(nc.vector.tensor_tensor(L[:, :, :], L[:, :, :],
                                                 gate_b[:, :].unsqueeze(1).to_broadcast([P, NT, E]), ALU.add))
                else:
                    link(nc.vector.tensor_reduce(m[0][:, :], L[:, :, :], AX.X, ALU.max))
                    nc.vector.tensor_tensor(t8[:, :, :], L[:, :, :],
                                            m[0][:, :].unsqueeze(2).to_broadcast([P, NT, E]),
                                            ALU.subtract).then_inc(logits_shifted, 1)
                    dve.wait_ge(exp_done, 1)
                    link(nc.vector.tensor_reduce(ind[:, :], u8[:, :, :], AX.X, ALU.add))
                    link(nc.vector.reciprocal(rank[:, :], ind[:, :]))
                    link(nc.vector.tensor_tensor(L[:, :, :], u8[:, :, :],
                                                 rank[:, :].unsqueeze(2).to_broadcast([P, NT, E]), ALU.mult))
                for k in range(2):
                    bc = m[k][:, :].unsqueeze(2).to_broadcast([P, NT, E])
                    link(nc.vector.tensor_reduce(m[k][:, :], L[:, :, :], AX.X, ALU.max))
                    link(nc.vector.tensor_tensor(t8[:, :, :], L[:, :, :], bc, ALU.is_lt))
                    link(nc.vector.scalar_tensor_tensor(out=t8[:, :, :], in0=t8[:, :, :], scalar=float(E),
                                                        in1=c.expert_id[:, :, :], op0=ALU.mult, op1=ALU.add))
                    link(nc.vector.tensor_reduce(ind[:, :], t8[:, :, :], AX.X, ALU.min))
                    link(nc.vector.tensor_tensor(oh[k][:, :, :], c.expert_id[:, :, :],
                                                 ind[:, :].unsqueeze(2).to_broadcast([P, NT, E]), ALU.is_equal))
                    if k == 0:
                        link(nc.vector.scalar_tensor_tensor(out=L[:, :, :], in0=oh[0][:, :, :], scalar=-3e38,
                                                            in1=L[:, :, :], op0=ALU.mult, op1=ALU.add))
                nc.vector.tensor_tensor(chosen[:, :, :], oh[0][:, :, :], oh[1][:, :, :], ALU.add).then_inc(chosen_ready, 1)
                if gated:
                    nc.vector.tensor_tensor(ind[:, :], m[1][:, :], m[0][:, :], ALU.subtract).then_inc(logits_shifted, 1)
                    dve.wait_ge(exp_done, 1)
                    link(nc.vector.tensor_scalar(keep[:, :], rank[:, :], 1.0, None, ALU.add))
                    link(nc.vector.reciprocal(keep[:, :], keep[:, :]))
                    link(nc.vector.tensor_scalar(weight[0][:, :], keep[:, :], 0.5, None, ALU.mult))
                    link(nc.vector.tensor_tensor(weight[1][:, :], weight[0][:, :], rank[:, :], ALU.mult))
                else:
                    link(nc.vector.tensor_tensor(ind[:, :], m[0][:, :], m[1][:, :], ALU.add))
                    link(nc.vector.reciprocal(keep[:, :], ind[:, :]))
                    for k in range(2):
                        link(nc.vector.scalar_tensor_tensor(out=weight[k][:, :], in0=m[k][:, :], scalar=0.5,
                                                            in1=keep[:, :], op0=ALU.mult, op1=ALU.mult))
                dve.wait_ge(counted, 1)
                for e in range(E):
                    link(nc.vector.tensor_tensor_scan(cum[:, e, :], c.ones_f[:, :], tot3[:, :, e], 0.0,
                                                      ALU.mult, ALU.add))
                link(nc.vector.tensor_copy(t8[:, :, :], pre3))
                link(nc.vector.tensor_tensor(u8[:, :, :], t8[:, :, :], tot3, ALU.subtract))
                link(nc.vector.tensor_tensor(u8[:, :, :], u8[:, :, :], cum[:, :, :].rearrange("p e t -> p t e"), ALU.add))
                if gated:
                    link(nc.vector.tensor_copy(cnt[:, :], cum[:, :, NT - 1]))
                else:
                    link(nc.vector.tensor_scalar(cnt[:, :], cum[:, :, NT - 1], float(CAP), None, ALU.min))
                link(nc.vector.tensor_scalar(cnt[:, :], cnt[:, :], float(BLK - 1), None, ALU.add))
                link(nc.vector.tensor_copy(cnt_i[:, :], cnt[:, :]))
                link(nc.vector.tensor_scalar(cnt_i[:, :], cnt_i[:, :], BLK.bit_length() - 1, BLK.bit_length() - 1,
                                             ALU.logical_shift_right, ALU.logical_shift_left))
                link(nc.vector.tensor_copy(cnt[:, :], cnt_i[:, :]))
                link(nc.vector.tensor_tensor_scan(run_end[:, :], c.ones_f[:, 0:E], cnt[:, :], 0.0, ALU.mult, ALU.add))
                link(nc.vector.tensor_tensor(run_base[:, :], run_end[:, :], cnt[:, :], ALU.subtract))
                for k in range(2):
                    link(nc.vector.tensor_tensor(t8[:, :, :], oh[k][:, :, :], u8[:, :, :], ALU.mult))
                    link(nc.vector.tensor_reduce(rank[:, :], t8[:, :, :], AX.X, ALU.add))
                    link(nc.vector.tensor_tensor(t8[:, :, :], oh[k][:, :, :],
                                                 run_base[:, :].unsqueeze(1).to_broadcast([P, NT, E]), ALU.mult))
                    link(nc.vector.tensor_reduce(base_k[:, :], t8[:, :, :], AX.X, ALU.add))
                    if gated:
                        link(nc.vector.tensor_tensor(put_i[k][:, :], rank[:, :], base_k[:, :], ALU.add))
                        link(nc.vector.tensor_copy(get_i[k][:, :], put_i[k][:, :]))
                        continue
                    link(nc.vector.tensor_scalar(keep[:, :], rank[:, :], float(CAP), None, ALU.is_lt))
                    link(nc.vector.tensor_tensor(weight[k][:, :], weight[k][:, :], keep[:, :], ALU.mult))
                    link(nc.vector.tensor_scalar(ind[:, :], rank[:, :], float(CAP - 1), None, ALU.min))
                    link(nc.vector.tensor_tensor(ind[:, :], ind[:, :], base_k[:, :], ALU.add))
                    link(nc.vector.tensor_copy(get_i[k][:, :], ind[:, :]))
                    link(nc.vector.tensor_scalar(ind[:, :], ind[:, :], c.drop_row[:, 0:1], None, ALU.subtract))
                    link(nc.vector.tensor_tensor(ind[:, :], ind[:, :], keep[:, :], ALU.mult))
                    link(nc.vector.tensor_scalar(put_i[k][:, :], ind[:, :], c.drop_row[:, 0:1], None, ALU.add))
                link(nc.vector.tensor_scalar(bmap[:, :], c.block_row[:, :], run_end[:, 0:1], None, ALU.is_ge))
                for e in range(1, E):
                    link(nc.vector.scalar_tensor_tensor(out=bmap[:, :], in0=c.block_row[:, :],
                                                        scalar=run_end[:, e:e + 1], in1=bmap[:, :],
                                                        op0=ALU.is_ge, op1=ALU.add))
                link(nc.vector.tensor_scalar(block_pack[:, :], bmap[:, :], float(E - 1), None, ALU.min))

            @block.tensor
            def _(pe):
                pe.wait_ge(gate_loaded, 48 if gated else 16)

                def logits(g, slot):
                    pe.wait_ge(centred, g * GRP + GRP)
                    wait(pe, copied, g - 1)
                    for k in range(GRP):
                        ins = nc.tensor.transpose(tps[slot][:, at(k, P)], xc[:, slot, k, :], c.ident[:, :])
                    ins.then_inc(transposed, 1)
                    pe.wait_ge(copied, g + 1)
                    for k in range(GRP):
                        ins = nc.tensor.matmul(lps[:, at(g * GRP + k, E)], xcT[:, slot, at(k, P)], gate_w[:, :],
                                               start=True, stop=True)
                    ins.then_inc(logits_done, 1)
                two_slot_loop(pe, NG, logits)
                pe.wait_ge(chosen_ready, 1)
                ch = chosen[:, :, :].rearrange("p t e -> p (t e)")
                nc.tensor.matmul(pre_ps[:, :], c.before[:, :], ch, start=True, stop=True)
                nc.tensor.matmul(tot_ps[:, :], c.ones_bf[:, :], ch, start=True, stop=True).then_inc(counted, 1)

            @block.scalar
            def _(act):
                def copy_out(g, slot):
                    act.wait_ge(transposed, g + 1)
                    wait(act, logits_done, g - 1)
                    nc.scalar.copy(xcT[:, slot, :], tps[slot][:, :]).then_inc(copied, 1)
                two_slot_loop(act, NG, copy_out)
                act.wait_ge(logits_shifted, 1)
                if gated:
                    nc.scalar.activation(rank[:, :], ind[:, :], ACT.Exp).then_inc(exp_done, 1)
                else:
                    nc.scalar.activation(u8[:, :, :], t8[:, :, :], ACT.Exp).then_inc(exp_done, 1)

        with ExitStack() as rc:
            stage = rc.enter_context(nc.sbuf_tensor(f"{tag}_stage", [P, 2, GRP, D], F32))
            stage_i = rc.enter_context(nc.sbuf_tensor(f"{tag}_stage_i", [P, 2, 2, GRP], I32))
            centred = nc.alloc_semaphore(f"{tag}_stage_centred")
            staged = nc.alloc_semaphore(f"{tag}_staged")
            index_staged = nc.alloc_semaphore(f"{tag}_index_staged")
            self_added = nc.alloc_semaphore(f"{tag}_self_added")
            begun = nc.alloc_semaphore(f"{tag}_put_begun")
            scattered = [nc.alloc_semaphore(f"{tag}_scattered{u}") for u in range(2)]
            if gated:
                xc = rc.enter_context(nc.sbuf_tensor(f"{tag}_stage_xc", [P, 2, GRP, D], F32))
            block = rc.enter_context(nc.Block())
            per = 2 * GRP * 16

            if gated:
                @block.scalar
                def _(act):
                    def fill(g, slot):
                        wait(act, scattered[slot], g // 2 * per)
                        act.wait_ge(centred, g * GRP + GRP)
                        for k in range(GRP):
                            nc.scalar.activation(stage[:, slot, k:k + 1, :], xc[:, slot, k:k + 1, :], ACT.Copy,
                                                 scale=rstd[:, at(g * GRP + k)]).then_inc(staged, 1)
                    two_slot_loop(act, NG, fill)

            @block.vector
            def _(dve):
                def fill(g, slot):
                    if gated:
                        wait(dve, staged, (g - 1) * GRP)
                    wait(dve, scattered[slot], g // 2 * per)
                    for k in range(GRP):
                        t = g * GRP + k
                        if gated:
                            nc.vector.scalar_tensor_tensor(
                                out=xc[:, slot, k:k + 1, :], in0=c.x[:, at(t), :], scalar=mean[:, at(t)],
                                in1=ln_w[:, :].unsqueeze(1), op0=ALU.subtract, op1=ALU.mult).then_inc(centred, 1)
                        else:
                            nc.vector.tensor_scalar(stage[:, slot, k:k + 1, :], c.x[:, at(t), :], mean[:, at(t)],
                                                    rstd[:, at(t)], ALU.subtract, ALU.mult).then_inc(staged, 1)
                    for k in range(2):
                        nc.vector.tensor_copy(stage_i[:, slot, k, :], put_i[k][:, at(g, GRP)]).then_inc(index_staged, 1)
                    if not gated:
                        dve.wait_ge(staged, g * GRP + GRP)
                        for k in range(GRP):
                            t = g * GRP + k
                            nc.vector.scalar_tensor_tensor(out=c.x[:, at(t), :], in0=stage[:, slot, k:k + 1, :], scalar=0.5,
                                                           in1=c.x[:, at(t), :], op0=ALU.mult, op1=ALU.add).then_inc(self_added, 1)
                two_slot_loop(dve, NG, fill)
                if not gated:
                    dve.wait_ge(self_added, NT)

            @block.gpsimd
            def _(pool):
                def put(g, slot):
                    pool.wait_ge(staged, g * GRP + GRP)
                    pool.wait_ge(index_staged, g * 2 + 2)
                    pool.sem_inc(begun, 1)
                    for j in range(GRP):
                        for k in range(2):
                            pool.indirect_dma_start(c.rows_in, bass.IndirectOffsetOnAxis(stage_i[:, slot, k, j:j + 1], 0),
                                                    stage[:, slot, j, :], None).then_inc(scattered[slot], 16)
                two_slot_loop(pool, NG, put)
                for u in range(2):
                    pool.wait_ge(scattered[u], NG // 2 * per)

        with ExitStack() as rc:
            def rsb(name, shape, dt=F32):
                return rc.enter_context(nc.sbuf_tensor(f"{tag}_{name}", shape, dt))

            def bank(name):
                return rc.enter_context(nc.psum_tensor(f"{tag}_{name}", [P, 2, BLK], F32))

            def rsem(name):
                return nc.alloc_semaphore(f"{tag}_{name}")
            rows = rsb("rows", [P, 2, 2, D])
            rowsT = rsb("rowsT", [D, 2, BLK])
            own = rsb("own", [P, 2, PACK])
            act_a = rsb("act_a", [P, 2, 2, BLK])
            hid = rsb("hid", [P, 2, FC, BLK])
            y_sb = rsb("y_sb", [P, 2, 2, D])
            T_ps = bank("T_ps")
            A_ps = [bank(f"A_ps{h}") for h in range(2)]
            B_ps = [bank(f"B_ps{h}") for h in range(2)] if gated else None
            Y_ps = [rc.enter_context(nc.psum_tensor(f"{tag}_Y_ps{u}", [P, 2, D], F32)) for u in range(2)]
            rows_loaded = [rsem(f"rows_loaded{u}") for u in range(2)]
            rows_used = rsem("rows_used")
            rowsT_ready = rsem("rowsT_ready")
            own_ready = rsem("own_ready")
            a_ready = rsem("a_ready")
            b_ready = rsem("b_ready")
            silu_ready = rsem("silu_ready")
            hid_ready = rsem("hid_ready")
            y_ready = rsem("y_ready")
            y_copied = rsem("y_copied")
            y_stored = [rsem(f"y_stored{u}") for u in range(2)]
            block = rc.enter_context(nc.Block())
            in_v = c.rows_in[0:ROWS, :].rearrange("(b p r) d -> b p (r d)", p=P, r=2)
            out_v = c.rows_out.rearrange("(b p r) d -> b p (r d)", p=P, r=2)

            def fills(b):
                return b // 2

            @block.sync
            def _(sp):
                def load(b, slot):
                    wait(sp, rows_used, b - 1)
                    sp.dma_start(rows[:, slot, :, :].rearrange("p r d -> p (r d)"),
                                 in_v[at(b), :, :].squeeze(0)).then_inc(rows_loaded[slot], 16)
                two_slot_loop(sp, NBLK, load)

            @block.tensor
            def _(pe):
                def turn(b, slot):
                    pe.wait_ge(rows_loaded[slot], fills(b) * 16 + 16)
                    wait(pe, rowsT_ready, b)
                    for r in range(2):
                        ins = nc.tensor.transpose(T_ps[:, r, 0:P], rows[:, slot, r, :], c.ident[:, :])
                    ins.then_inc(rows_used, 1)

                def up(b, slot, h):
                    for j in range(2):
                        f = 2 * h + j
                        ins = nc.tensor.matmul(A_ps[h][:, j, :], own[:, slot, W1A + f * P:W1A + (f + 1) * P],
                                               rowsT[:, slot, :], start=True, stop=True)
                    ins.then_inc(a_ready, 1)
                    if gated:
                        for j in range(2):
                            f = 2 * h + j
                            ins = nc.tensor.matmul(B_ps[h][:, j, :], own[:, slot, W1B + f * P:W1B + (f + 1) * P],
                                                   rowsT[:, slot, :], start=True, stop=True)
                        ins.then_inc(b_ready, 1)

                def down(b, slot):
                    pe.wait_ge(hid_ready, b * 2 + 2)
                    wait(pe, y_copied, b - 1)
                    for r in range(2):
                        for f in range(FC):
                            ins = nc.tensor.matmul(Y_ps[slot][:, r, :], hid[:, slot, f, at(r, P)],
                                                   own[:, slot, W2 + f * D:W2 + (f + 1) * D],
                                                   start=(f == 0), stop=(f == FC - 1))
                    ins.then_inc(y_ready, 1)

                def step(b, slot, first=False, last=False):
                    pe.wait_ge(rowsT_ready, b + 1)
                    pe.wait_ge(own_ready, b + 1)
                    wait(pe, hid_ready, b * 2 - 1)
                    up(b, slot, 0)
                    if not last:
                        turn(b + 1, 1 - slot)
                    if not first:
                        down(b - 1, 1 - slot)
                    up(b, slot, 1)
                turn(0, 0)
                step(0, 0, first=True)
                step(1, 1)
                with pe.Fori(0, (NBLK - 4) // 2) as i:
                    step(i * 2 + 2, 0)
                    step(i * 2 + 3, 1)
                step(NBLK - 2, 0)
                step(NBLK - 1, 1, last=True)
                down(NBLK - 1, 1)

            @block.scalar
            def _(act):
                def turned(b, slot):
                    act.wait_ge(rows_used, b + 1)
                    wait(act, a_ready if not gated else b_ready, b * 2 - 2)
                    nc.scalar.copy(rowsT[:, slot, :].rearrange("p (r q) -> p r q", r=2), T_ps[:, :, 0:P]).then_inc(rowsT_ready, 1)

                def silu(b, slot, h):
                    act.wait_ge(a_ready, b * 2 + h + 1)
                    if gated:
                        wait(act, hid_ready, b * 2 + h - 1)
                        for j in range(2):
                            f = 2 * h + j
                            ins = nc.scalar.activation(act_a[:, h, j, :], A_ps[h][:, j, :], ACT.Silu,
                                                       bias=own[:, slot, B1A + f:B1A + f + 1])
                        ins.then_inc(silu_ready, 1)
                    else:
                        wait(act, y_ready, b - 1)
                        nc.scalar.activation(hid[:, slot, 2 * h:2 * h + 2, :], A_ps[h][:, :, :], ACT.Silu).then_inc(hid_ready, 1)

                def step(b, slot, last=False):
                    silu(b, slot, 0)
                    if not last:
                        turned(b + 1, 1 - slot)
                    silu(b, slot, 1)
                turned(0, 0)
                step(0, 0)
                step(1, 1)
                with act.Fori(0, (NBLK - 4) // 2) as i:
                    step(i * 2 + 2, 0)
                    step(i * 2 + 3, 1)
                step(NBLK - 2, 0)
                step(NBLK - 1, 1, last=True)

            @block.vector
            def _(dve):
                def select(b, slot):
                    wait(dve, y_ready, b - 1)
                    if gated:
                        wait(dve, y_copied, b - 1)
                        wait(dve, hid_ready, b * 2 - 2)
                    wait(dve, own_ready, b)
                    e = dve.value_load(block_pack[0:1, at(b)], min_val=0, max_val=E - 1)
                    nc.vector.tensor_copy(own[:, slot, :], packs[:, bass.ds(e, 1), :].squeeze(1)).then_inc(own_ready, 1)

                def mul(b, slot, h):
                    dve.wait_ge(silu_ready, b * 2 + h + 1)
                    dve.wait_ge(b_ready, b * 2 + h + 1)
                    wait(dve, y_ready, b - 1)
                    for j in range(2):
                        f = 2 * h + j
                        ins = nc.vector.scalar_tensor_tensor(
                            out=hid[:, slot, f, :], in0=B_ps[h][:, j, :], scalar=own[:, slot, B1B + f:B1B + f + 1],
                            in1=act_a[:, h, j, :], op0=ALU.add, op1=ALU.mult)
                    ins.then_inc(hid_ready, 1)

                def finish(b, slot):
                    dve.wait_ge(y_ready, b + 1)
                    wait(dve, y_stored[slot], fills(b) * 16)
                    if gated:
                        nc.vector.tensor_tensor(y_sb[:, slot, :, :], Y_ps[slot][:, :, :],
                                                own[:, slot, B2:B2 + D].unsqueeze(1).to_broadcast([P, 2, D]),
                                                ALU.add).then_inc(y_copied, 1)
                    else:
                        nc.vector.tensor_copy(y_sb[:, slot, :, :], Y_ps[slot][:, :, :]).then_inc(y_copied, 1)

                def step(b, slot, first=False, last=False):
                    if gated:
                        mul(b, slot, 0)
                    if not first:
                        finish(b - 1, 1 - slot)
                    if not last:
                        select(b + 1, 1 - slot)
                    if gated:
                        mul(b, slot, 1)
                dve.wait_ge(w_loaded, w["n_loads"] * 16)
                select(0, 0)
                step(0, 0, first=True)
                step(1, 1)
                with dve.Fori(0, (NBLK - 4) // 2) as i:
                    step(i * 2 + 2, 0)
                    step(i * 2 + 3, 1)
                step(NBLK - 2, 0)
                step(NBLK - 1, 1, last=True)
                finish(NBLK - 1, 1)

            @block.gpsimd
            def _(pool):
                def store(b, slot):
                    pool.wait_ge(y_copied, b + 1)
                    pool.dma_start(out_v[at(b), :, :].squeeze(0),
                                   y_sb[:, slot, :, :].rearrange("p r d -> p (r d)")).then_inc(y_stored[slot], 16)
                two_slot_loop(pool, NBLK, store)
                for u in range(2):
                    pool.wait_ge(y_stored[u], NBLK // 2 * 16)

        with ExitStack() as rc:
            got = rc.enter_context(nc.sbuf_tensor(f"{tag}_got", [P, 2, 2, GRP, D], F32))
            stage_i = rc.enter_context(nc.sbuf_tensor(f"{tag}_stage_g", [P, 2, 2, GRP], I32))
            index_staged = nc.alloc_semaphore(f"{tag}_gindex_staged")
            begun = nc.alloc_semaphore(f"{tag}_get_begun")
            gathered = [nc.alloc_semaphore(f"{tag}_gathered{u}") for u in range(2)]
            added = nc.alloc_semaphore(f"{tag}_added")
            block = rc.enter_context(nc.Block())
            per = 2 * GRP * 16

            @block.gpsimd
            def _(pool):
                def get(g, slot):
                    pool.wait_ge(index_staged, g * 2 + 2)
                    wait(pool, added, (g - 1) * 2 * GRP)
                    pool.sem_inc(begun, 1)
                    for j in range(GRP):
                        for k in range(2):
                            pool.indirect_dma_start(got[:, slot, k, j, :], None, c.rows_out,
                                                    bass.IndirectOffsetOnAxis(stage_i[:, slot, k, j:j + 1], 0)
                                                    ).then_inc(gathered[slot], 16)
                two_slot_loop(pool, NG, get)

            @block.vector
            def _(dve):
                def fill(g, slot):
                    wait(dve, gathered[slot], (g // 2) * per)
                    for k in range(2):
                        nc.vector.tensor_copy(stage_i[:, slot, k, :], get_i[k][:, at(g, GRP)]).then_inc(index_staged, 1)

                def add(g, slot, last=False):
                    if not last:
                        fill(g + 1, 1 - slot)
                    dve.wait_ge(gathered[slot], (g // 2) * per + per)
                    for k in range(2):
                        for j in range(GRP):
                            t = g * GRP + j
                            nc.vector.scalar_tensor_tensor(
                                out=c.x[:, at(t), :], in0=got[:, slot, k, j, :].unsqueeze(1), scalar=weight[k][:, at(t)],
                                in1=c.x[:, at(t), :], op0=ALU.mult, op1=ALU.add).then_inc(added, 1)
                        if k == 0:
                            dve.wait_ge(added, g * 2 * GRP + GRP)
                fill(0, 0)
                add(0, 0)
                add(1, 1)
                with dve.Fori(0, (NG - 4) // 2) as i:
                    add(i * 2 + 2, 0)
                    add(i * 2 + 3, 1)
                add(NG - 2, 0)
                add(NG - 1, 1, last=True)


def scan_layer(nc, c, tag, selective, w):
    NS = 16
    HC = SEQ // 512
    PAIR = 2 * NS
    ALLN = HALVES * NS
    with ExitStack() as ctx:
        def sb(name, shape, dt=F32):
            return ctx.enter_context(nc.sbuf_tensor(f"{tag}_{name}", shape, dt))

        def sem(name):
            return nc.alloc_semaphore(f"{tag}_{name}")

        mean = sb("mean", [P, NT])
        rstd = sb("rstd", [P, NT])
        row_statistics(nc, c, tag, mean, rstd, False)

        w_in = sb("w_in", [D, 2 * INNER])
        w_out = sb("w_out", [P, HALVES, D])
        taps = sb("taps", [P, HALVES, CONV])
        d_skip = sb("d_skip", [P, HALVES])
        dt_b = sb("dt_b", [P, HALVES])
        xn = sb("xn", [P, SEQ // P, D])
        xnT = sb("xnT", [D, SEQ])
        xpad = sb("xpad", [P, HALVES, CONV - 1 + SEQ])
        conv = sb("conv", [P, HALVES, SEQ])
        u = [sb(f"u{i}", [P, HALVES, SEQ]) for i in range(2)]
        z = [sb(f"z{i}", [P, HALVES, SEQ]) for i in range(2)]
        y = sb("y", [P, HALVES, SEQ])
        e = y
        loaded = sem("loaded")
        cleared = sem("cleared")
        if selective:
            conv_b = sb("conv_b", [P, HALVES])
            w_rank = sb("w_rank", [P, HALVES, PAIR])
            w_bc = sb("w_bc", [P, HALVES, 2, 3 * PAIR])
            w_dt = sb("w_dt", [PAIR, HALVES, P])
            decay = sb("decay", [P, HALVES, NS])
            pick = sb("pick", [3 * PAIR, NS, P], BF16)
            rank = sb("rank", [PAIR, HALVES, SEQ])
            delta = sb("delta", [P, HALVES, SEQ])
            du = sb("du", [P, HALVES, SEQ])
            parts = sb("parts", [3 * PAIR, HALVES, 2, SEQ], BF16)
            work = sb("work", [P, 8, SEQ])
            dA, Bs, dBu = ([work[:, 2 * i + k, :] for k in range(2)] for i in range(3))
            prod = [work[:, 6 + k, :] for k in range(2)]
            st = [sb(f"st{k}", [P, SEQ]) for k in range(2)]
            rest = [prod[k][0:3 * PAIR, 0:512] for k in range(2)]
            mid = sb("mid", [3 * PAIR, 2, 512], BF16)
            log1p = du
            b_ps = ctx.enter_context(nc.psum_tensor(f"{tag}_b_ps", [P, SEQ], F32))
            c_ps = ctx.enter_context(nc.psum_tensor(f"{tag}_c_ps", [P, SEQ], F32))
            y_ps = ctx.enter_context(nc.psum_tensor(f"{tag}_y_ps", [P, SEQ], F32))
        else:
            w_x = sb("w_x", [P, HALVES, PAIR])
            w_dt = sb("w_dt", [PAIR, INNER])
            w_b = sb("w_b", [PAIR, INNER])
            xp = sb("xp", [PAIR, SEQ])
            keep = sb("keep", [P, HALVES, SEQ])
            ub = sb("ub", [P, HALVES, SEQ])
        banks = [ctx.enter_context(nc.psum_tensor(f"{tag}_bank{i}", [P, 512], F32)) for i in range(2)]
        full = [sem(f"bank{i}_full") for i in range(2)]
        free = [sem(f"bank{i}_free") for i in range(2)]
        xn_ready, xpad_ready, conv_step, conv_ready = sem("xn_ready"), sem("xpad_ready"), sem("conv_step"), sem("conv_ready")
        u_ready, y_ready, y_gated, scanned, soft_step, log_ready = (
            sem("u_ready"), sem("y_ready"), sem("y_gated"), sem("scanned"), sem("soft_step"), sem("log_ready"))

        if selective:
            pick_step, decay_step, abs_ready, du_ready = sem("pick_step"), sem("decay_step"), sem("abs_ready"), sem("du_ready")
            hi_ready, mid_done, mid_ready, parts_ready = sem("hi_ready"), sem("mid_done"), sem("mid_ready"), sem("parts_ready")
            b_full, c_full, dA_ready, Bs_ready = sem("b_full"), sem("c_full"), sem("dA_ready"), sem("Bs_ready")
            dBu_ready, prod_ready, prod_used = sem("dBu_ready"), sem("prod_ready"), sem("prod_used")
        else:
            exp_ready = sem("exp_ready")

        FRONT, BACK = 10, 2
        MID = 16 if selective else 10
        TURN = FRONT + MID + BACK

        def front_use(s, k):
            return k if isinstance(s, int) and s == 0 else s * TURN - MID - BACK + k

        def middle_use(s, k):
            return s * TURN + (FRONT if isinstance(s, int) and s == SEQS - 1 else 2 * FRONT) + k

        def back_use(s, k):
            return middle_use(s, MID) + k

        class Use:
            def __init__(self, section, s, k):
                start = section(s, 0)
                self.bank = k % 2
                if isinstance(start, int):
                    self.before = start // 2 + k // 2
                else:
                    self.before = s * (TURN // 2) + (section(1, 0) - TURN) // 2 + k // 2
                self.ps, self.full, self.free = banks[self.bank], full[self.bank], free[self.bank]

            def fill(self, pe):
                wait(pe, self.free, self.before)

            def read(self, eng):
                eng.wait_ge(self.full, self.before + 1)

            def taken(self, eng):
                eng.wait_ge(self.free, self.before + 1)

        def order(eng, front, rest):
            front(0, 0)
            front(1, 1)
            rest(0, 0)
            with eng.Fori(0, (SEQS - 2) // 2) as i:
                front(i * 2 + 2, 0)
                rest(i * 2 + 1, 1)
                front(i * 2 + 3, 1)
                rest(i * 2 + 2, 0)
            rest(SEQS - 1, 1)

        LOADS = 16 * (5 + 2 + HALVES * 2 * (2 + 2 * 3) if selective else 5 + 3)
        block = ctx.enter_context(nc.Block())

        @block.sync
        def _(sp):
            def load(dst, src, **kw):
                sp.dma_start(dst, src, **kw).then_inc(loaded, 16)
            load(w_in[:, :], w["w_in"])
            load(w_out[:, :, :], w["w_out"].rearrange("(h p) d -> p h d", p=P))
            load(taps[:, :, :], w["conv_w"].rearrange("(h p) o k -> p h (o k)", p=P))
            load(d_skip[:, :], w["d_skip"].rearrange("(h p) -> p h", p=P), allow_slow_non_contiguous=True)
            load(dt_b[:, :], w["dt_b"].rearrange("(h p) -> p h", p=P), allow_slow_non_contiguous=True)
            if not selective:
                load(w_x[:, :, :], w["w_x"].rearrange("(h p) r -> p h r", p=P))
                sp.wait_ge(cleared, 3)
                load(w_dt[0:NS, :], w["w_dt"])
                load(w_b[NS:PAIR, :], w["w_b"])
            else:
                load(conv_b[:, :], w["conv_b"].rearrange("(h p) -> p h", p=P), allow_slow_non_contiguous=True)
                load(decay[:, :, :], w["a_log"].rearrange("(h p) n -> p h n", p=P))
                sp.wait_ge(cleared, 4)
                for h in range(HALVES):
                    for j in range(2):
                        head, rows, cols = 2 * h + j, at(j, P // 2), at(j, NS)
                        load(w_rank[rows, h, cols], w["w_x"][:, head, 0:NS])
                        load(w_dt[cols, h, rows], w["w_dt"][:, head, :])
                        for k in range(2):
                            for part in range(3):
                                first = part * PAIR + j * NS
                                load(w_bc[rows, h, k, first:first + NS], w["w_x"][:, head, at(k + 1, NS)])


        @block.gpsimd
        def _(pool):
            nc.gpsimd.memset(xpad[:, :, 0:CONV - 1], 0.0).then_inc(cleared, 1)
            if not selective:
                nc.gpsimd.memset(w_b[:, :], 0.0).then_inc(cleared, 1)
                nc.gpsimd.memset(w_dt[:, :], 0.0).then_inc(cleared, 1)
            else:
                for t in (w_rank[:, :, :], w_bc[:, :, :, :], w_dt[:, :, :]):
                    nc.gpsimd.memset(t, 0.0).then_inc(cleared, 1)
                link = chain(pool, pick_step)
                link(nc.gpsimd.memset(pick[:, :, :], 0.0))
                for part in range(3):
                    for j in range(2):
                        cell = pick[:, :, at(j, P // 2)]
                        link(nc.gpsimd.affine_select(out=cell, in_=cell, compare_op=ALU.not_equal, fill=1.0,
                                                     base=-(part * PAIR + j * NS), pattern=[[-1, NS], [0, P // 2]],
                                                     channel_multiplier=1))

            def rest_of(s, slot):
                if selective:
                    pool.wait_ge(soft_step, s * 4 + 4)
                    pool.wait_ge(u_ready, s * HALVES + HALVES)
                    nc.gpsimd.tensor_tensor(du[:, :, :], delta[:, :, :], u[slot][:, :, :], ALU.mult).then_inc(du_ready, 1)
                    pool.wait_ge(du_ready, s + 1)
                    for h in range(HALVES):
                        def input_of(n, k):
                            q = s * ALLN + h * NS + n
                            pool.wait_ge(Bs_ready, q + 1)
                            wait(pool, scanned, q - 1) if isinstance(q, int) else pool.wait_ge(scanned, q - 1)
                            nc.gpsimd.tensor_tensor(dBu[k], du[:, h, :], Bs[k], ALU.mult).then_inc(dBu_ready, 1)
                        input_of(0, 0)
                        input_of(1, 1)
                        with pool.Fori(0, (NS - 2) // 2) as i:
                            input_of(i * 2 + 2, 0)
                            input_of(i * 2 + 3, 1)
                pool.wait_ge(y_ready, s * HALVES + HALVES)
                for k in (FRONT - 2, FRONT - 1):
                    Use(front_use, s, k).taken(pool)
                nc.gpsimd.tensor_tensor(y[:, :, :], y[:, :, :], z[slot][:, :, :], ALU.mult).then_inc(y_gated, 1)
            order(pool, lambda s, slot: None, rest_of)

        @block.tensor
        def _(pe):
            pe.wait_ge(loaded, LOADS)
            if selective:
                pe.wait_ge(pick_step, 7)

            def front(s, slot):
                pe.wait_ge(xn_ready, s * 8 + 8)
                for g in range(2):
                    use = Use(front_use, s, g)
                    use.fill(pe)
                    for k in range(GRP):
                        ins = nc.tensor.transpose(use.ps[:, at(k, P)], xn[:, g * GRP + k, :], c.ident[:, :])
                    ins.then_inc(use.full, 1)
                for g in range(2):
                    Use(front_use, s, g).taken(pe)
                for m in range(2 * HALVES):
                    for cc in range(HC):
                        use = Use(front_use, s, 2 + m * HC + cc)
                        use.fill(pe)
                        nc.tensor.matmul(use.ps[:, :], w_in[:, at(m, P)], xnT[:, at(cc, 512)],
                                         start=True, stop=True).then_inc(use.full, 1)

            def rest_of(s, slot):
                pe.wait_ge(u_ready, s * HALVES + HALVES)
                k = 0
                if not selective:
                    for cc in range(HC):
                        use = Use(middle_use, s, k)
                        k += 1
                        use.fill(pe)
                        for h in range(HALVES):
                            ins = nc.tensor.matmul(use.ps[0:PAIR, :], w_x[:, h, :], u[slot][:, h, at(cc, 512)],
                                                   start=(h == 0), stop=(h == HALVES - 1))
                        ins.then_inc(use.full, 1)
                    for cc in range(HC):
                        Use(middle_use, s, cc).taken(pe)
                    for wt in (w_dt, w_b):
                        for h in range(HALVES):
                            for cc in range(HC):
                                use = Use(middle_use, s, k)
                                k += 1
                                use.fill(pe)
                                nc.tensor.matmul(use.ps[:, :], wt[:, at(h, P)], xp[:, at(cc, 512)],
                                                 start=True, stop=True).then_inc(use.full, 1)
                else:
                    for h in range(HALVES):
                        for cc in range(HC):
                            use = Use(middle_use, s, k)
                            k += 1
                            use.fill(pe)
                            nc.tensor.matmul(use.ps[0:PAIR, :], w_rank[:, h, :], u[slot][:, h, at(cc, 512)],
                                             start=True, stop=True).then_inc(use.full, 1)
                    for j in (2, 3):
                        Use(middle_use, s, j).taken(pe)
                    for h in range(HALVES):
                        for cc in range(HC):
                            use = Use(middle_use, s, k)
                            k += 1
                            use.fill(pe)
                            nc.tensor.matmul(use.ps[:, :], w_dt[:, h, :], rank[:, h, at(cc, 512)],
                                             start=True, stop=True).then_inc(use.full, 1)
                    for h in range(HALVES):
                        for kind in range(2):
                            for cc in range(HC):
                                use = Use(middle_use, s, k)
                                k += 1
                                use.fill(pe)
                                nc.tensor.matmul(use.ps[0:3 * PAIR, :], w_bc[:, h, kind, :], u[slot][:, h, at(cc, 512)],
                                                 start=True, stop=True).then_inc(use.full, 1)
                    pe.wait_ge(parts_ready, s * 8 + 8)
                    for h in range(HALVES):
                        def q_of(n):
                            return s * ALLN + h * NS + n

                        def spread(ps, kind, n, done, freed, count):
                            wait(pe, freed, count)
                            for cc in range(HC):
                                ins = nc.tensor.matmul(ps[:, at(cc, 512)], pick[:, at(n), :].squeeze(1) if not isinstance(n, int) else pick[:, n, :],
                                                       parts[:, h, kind, at(cc, 512)], start=True, stop=True)
                            ins.then_inc(done, 1)

                        def gather_y(n, k, start=False, stop=False):
                            pe.wait_ge(prod_ready, q_of(n) + 1)
                            for cc in range(HC):
                                ins = nc.tensor.matmul(y_ps[:, at(cc, 512)], c.ident[:, :], prod[k][:, at(cc, 512)],
                                                       start=start, stop=stop)
                            ins.then_inc(prod_used, 1)

                        def step(n, k):
                            spread(c_ps, 1, n, c_full, prod_ready, q_of(n))
                            if not (isinstance(n, int) and n == NS - 1):
                                spread(b_ps, 0, n + 1, b_full, Bs_ready, q_of(n) + 1)
                            if not (isinstance(n, int) and n == 0):
                                gather_y(n - 1, 1 - k, start=isinstance(n, int) and n == 1)
                        spread(b_ps, 0, 0, b_full, Bs_ready, q_of(0))
                        wait(pe, y_ready, s * HALVES + h)
                        step(0, 0)
                        step(1, 1)
                        with pe.Fori(0, (NS - 4) // 2) as i:
                            step(i * 2 + 2, 0)
                            step(i * 2 + 3, 1)
                        step(NS - 2, 0)
                        step(NS - 1, 1)
                        gather_y(NS - 1, 1, stop=True)
                pe.wait_ge(y_gated, s + 1)
                for g in range(2):
                    use = Use(back_use, s, g)
                    use.fill(pe)
                    for j in range(GRP):
                        for h in range(HALVES):
                            ins = nc.tensor.matmul(use.ps[:, at(j, P)], y[:, h, at(g * GRP + j, P)], w_out[:, h, :],
                                                   start=(h == 0), stop=(h == HALVES - 1))
                    ins.then_inc(use.full, 1)
            order(pe, front, rest_of)

        @block.scalar
        def _(act):
            act.wait_ge(loaded, LOADS)
            act.wait_ge(cleared, 1)
            if selective:
                nc.scalar.activation(decay[:, :, :], decay[:, :, :], ACT.Exp).then_inc(decay_step, 1)
                act.wait_ge(decay_step, 1)
                nc.scalar.mul(decay[:, :, :], decay[:, :, :], -1.0).then_inc(decay_step, 1)
                act.wait_ge(decay_step, 2)

            def front(s, slot):
                for g in range(2):
                    use = Use(front_use, s, g)
                    use.read(act)
                    nc.scalar.copy(xnT[:, at(g, 512)], use.ps[:, :]).then_inc(use.free, 1)
                wait(act, conv_ready, s * HALVES)
                wait(act, u_ready, s * HALVES)
                for m in range(HALVES):
                    for cc in range(HC):
                        use = Use(front_use, s, 2 + m * HC + cc)
                        use.read(act)
                        nc.scalar.copy(xpad[:, m, CONV - 1 + cc * 512:CONV - 1 + (cc + 1) * 512], use.ps[:, :]).then_inc(xpad_ready, 1)
                        nc.scalar.activation(conv[:, m, at(cc, 512)], use.ps[:, :], ACT.Copy,
                                             scale=taps[:, m, CONV - 1:CONV]).then_inc(use.free, 1)
                wait(act, y_gated, s - 1)
                for m in range(HALVES):
                    for cc in range(HC):
                        use = Use(front_use, s, 2 + (HALVES + m) * HC + cc)
                        use.read(act)
                        nc.scalar.activation(z[slot][:, m, at(cc, 512)], use.ps[:, :], ACT.Silu).then_inc(use.free, 1)
                wait(act, y_ready, (s - 1) * HALVES)
                for m in range(HALVES):
                    act.wait_ge(conv_ready, s * HALVES + m + 1)
                    nc.scalar.activation(u[slot][:, m, :], conv[:, m, :], ACT.Silu,
                                         bias=conv_b[:, m:m + 1] if selective else 0.0).then_inc(u_ready, 1)

            def rest_of(s, slot):
                k = 0
                if not selective:
                    for cc in range(HC):
                        use = Use(middle_use, s, k)
                        k += 1
                        use.read(act)
                        nc.scalar.copy(xp[:, at(cc, 512)], use.ps[0:PAIR, :]).then_inc(use.free, 1)
                    for j in (HC + 2, HC + 3):
                        Use(middle_use, s, j).taken(act)
                    nc.scalar.activation(keep[:, :, :], keep[:, :, :], ACT.Exp).then_inc(exp_ready, 1)
                    act.wait_ge(exp_ready, s + 1)
                    nc.scalar.activation(keep[:, :, :], keep[:, :, :], ACT.Ln, bias=1.0).then_inc(log_ready, 1)
                    return
                for h in range(HALVES):
                    for cc in range(HC):
                        use = Use(middle_use, s, k)
                        k += 1
                        use.read(act)
                        nc.scalar.copy(rank[:, h, at(cc, 512)], use.ps[0:PAIR, :]).then_inc(use.free, 1)
                wait(act, scanned, s * ALLN)
                for h in range(HALVES):
                    for cc in range(HC):
                        use = Use(middle_use, s, k)
                        k += 1
                        use.read(act)
                        nc.scalar.activation(e[:, h, at(cc, 512)], use.ps[:, :], ACT.Abs, bias=dt_b[:, h:h + 1]).then_inc(abs_ready, 1)
                        nc.scalar.activation(delta[:, h, at(cc, 512)], use.ps[:, :], ACT.Relu, bias=dt_b[:, h:h + 1]).then_inc(use.free, 1)
                act.wait_ge(abs_ready, s * 5 + 4)
                nc.scalar.activation(e[:, :, :], e[:, :, :], ACT.Exp, scale=-1.0).then_inc(abs_ready, 1)
                act.wait_ge(abs_ready, s * 5 + 5)
                nc.scalar.activation(log1p[:, :, :], e[:, :, :], ACT.Ln, bias=1.0).then_inc(log_ready, 1)
                for j in range(8):
                    use = Use(middle_use, s, k + j)
                    use.read(act)
                    h, kind, cc = j // 4, j // 2 % 2, j % 2
                    nc.scalar.copy(parts[:, h, kind, at(cc, 512)], use.ps[0:3 * PAIR, :]).then_inc(hi_ready, 1)
                    if j > 0:
                        middle_part(act, s, j - 1)
                middle_part(act, s, 7)
                for h in range(HALVES):
                    def q_of(n):
                        return s * ALLN + h * NS + n

                    def step(n, k):
                        q = q_of(n)
                        wait(act, scanned, q - 1)
                        if isinstance(n, int) and n == 0 and h == 0:
                            act.wait_ge(soft_step, s * 4 + 4)
                        sc = decay[:, h, at(n)] if not isinstance(n, int) else decay[:, h, n:n + 1]
                        nc.scalar.activation(dA[k], delta[:, h, :], ACT.Exp, scale=sc).then_inc(dA_ready, 1)
                        act.wait_ge(b_full, q + 1)
                        wait(act, dBu_ready, q - 1)
                        nc.scalar.copy(Bs[k], b_ps[:, :]).then_inc(Bs_ready, 1)
                    step(0, 0)
                    step(1, 1)
                    with act.Fori(0, (NS - 2) // 2) as i:
                        step(i * 2 + 2, 0)
                        step(i * 2 + 3, 1)

            def middle_part(act, s, j):
                Use(middle_use, s, 8 + j).taken(act)
                h, kind, cc = j // 4, j // 2 % 2, j % 2
                nc.scalar.copy(parts[PAIR:2 * PAIR, h, kind, at(cc, 512)], rest[j % 2][PAIR:2 * PAIR, :]).then_inc(mid_ready, 1)
            order(act, front, rest_of)

        @block.vector
        def _(dve):
            dve.wait_ge(loaded, LOADS)

            def front(s, slot):
                if not (isinstance(s, int) and s == 0):
                    Use(front_use, s - 1, 1).read(dve)
                for j in range(SEQ // P):
                    t = s * (SEQ // P) + j
                    nc.vector.tensor_scalar(xn[:, j:j + 1, :], c.x[:, at(t), :], mean[:, at(t)], rstd[:, at(t)],
                                            ALU.subtract, ALU.mult).then_inc(xn_ready, 1)
                for m in range(HALVES):
                    for cc in range(HC):
                        Use(front_use, s, 2 + m * HC + cc).taken(dve)
                    dve.wait_ge(xpad_ready, s * HALVES * HC + (m + 1) * HC)
                    for k in range(CONV - 2, -1, -1):
                        ins = nc.vector.scalar_tensor_tensor(out=conv[:, m, :], in0=xpad[:, m, k:k + SEQ],
                                                             scalar=taps[:, m, k:k + 1], in1=conv[:, m, :],
                                                             op0=ALU.mult, op1=ALU.add)
                        if k > 0:
                            ins.then_inc(conv_step, 1)
                            dve.wait_ge(conv_step, s * 4 + m * 2 + (CONV - 1 - k))
                    ins.then_inc(conv_ready, 1)

            def rest_of(s, slot):
                k = 0
                if not selective:
                    k = HC
                    for h in range(HALVES):
                        for cc in range(HC):
                            use = Use(middle_use, s, k)
                            k += 1
                            use.read(dve)
                            nc.vector.tensor_scalar(keep[:, h, at(cc, 512)], use.ps[:, :], dt_b[:, h:h + 1], 20.0,
                                                    ALU.add, ALU.min).then_inc(use.free, 1)
                    for h in range(HALVES):
                        for cc in range(HC):
                            use = Use(middle_use, s, k)
                            k += 1
                            use.read(dve)
                            nc.vector.tensor_tensor(ub[:, h, at(cc, 512)], use.ps[:, :], u[slot][:, h, at(cc, 512)],
                                                    ALU.mult).then_inc(use.free, 1)
                    for j in (MID - 2, MID - 1):
                        Use(middle_use, s, j).taken(dve)
                    dve.wait_ge(log_ready, s + 1)
                    nc.vector.tensor_scalar(keep[:, :, :], keep[:, :, :], -1.0, 1.0, ALU.mult, ALU.add).then_inc(soft_step, 1)
                    dve.wait_ge(soft_step, s * 2 + 1)
                    nc.vector.tensor_scalar(keep[:, :, :], keep[:, :, :], 0.0, float(np.float32(1) - np.float32(1e-4)),
                                            ALU.max, ALU.min).then_inc(soft_step, 1)
                    dve.wait_ge(soft_step, s * 2 + 2)
                    for h in range(HALVES):
                        nc.vector.tensor_tensor_scan(y[:, h, :], keep[:, h, :], ub[:, h, :], 0.0,
                                                     ALU.mult, ALU.add).then_inc(scanned, 1)
                    for h in range(HALVES):
                        dve.wait_ge(scanned, s * HALVES + h + 1)
                        nc.vector.scalar_tensor_tensor(out=y[:, h, :], in0=u[slot][:, h, :], scalar=d_skip[:, h:h + 1],
                                                       in1=y[:, h, :], op0=ALU.mult, op1=ALU.add).then_inc(y_ready, 1)
                else:
                    k = 8
                    for j in range(8):
                        use = Use(middle_use, s, k + j)
                        h, kind, cc = j // 4, j // 2 % 2, j % 2
                        low = slice(2 * PAIR, 3 * PAIR)
                        dve.wait_ge(hi_ready, s * 8 + j + 1)
                        if j >= 2:
                            dve.wait_ge(mid_ready, s * 8 + j - 1)
                        nc.vector.tensor_tensor(rest[j % 2], use.ps[0:3 * PAIR, :], parts[:, h, kind, at(cc, 512)],
                                                ALU.subtract).then_inc(use.free, 1)
                        use.taken(dve)
                        nc.vector.tensor_copy(mid[low, j % 2, :], rest[j % 2][low, :]).then_inc(mid_done, 1)
                        dve.wait_ge(mid_done, s * 8 + j + 1)
                        nc.vector.tensor_tensor(parts[low, h, kind, at(cc, 512)], rest[j % 2][low, :], mid[low, j % 2, :],
                                                ALU.subtract).then_inc(parts_ready, 1)
                        dve.wait_ge(parts_ready, s * 8 + j + 1)
                    dve.wait_ge(mid_ready, s * 8 + 8)
                    dve.wait_ge(abs_ready, s * 5 + 5)
                    w1 = work[:, 0:2, :]
                    nc.vector.tensor_scalar(w1, e[:, :, :], 1.0, -1.0, ALU.add, ALU.add).then_inc(soft_step, 1)
                    dve.wait_ge(soft_step, s * 4 + 1)
                    dve.wait_ge(log_ready, s + 1)
                    nc.vector.tensor_tensor(e[:, :, :], e[:, :, :], w1, ALU.subtract).then_inc(soft_step, 1)
                    dve.wait_ge(soft_step, s * 4 + 2)
                    nc.vector.tensor_tensor(e[:, :, :], e[:, :, :], log1p[:, :, :], ALU.add).then_inc(soft_step, 1)
                    dve.wait_ge(soft_step, s * 4 + 3)
                    for j in (6, 7):
                        Use(middle_use, s, j).taken(dve)
                    nc.vector.tensor_tensor(delta[:, :, :], delta[:, :, :], e[:, :, :], ALU.add).then_inc(soft_step, 1)
                    for h in range(HALVES):
                        def step(n, k):
                            q = s * ALLN + h * NS + n
                            dve.wait_ge(dA_ready, q + 1)
                            dve.wait_ge(dBu_ready, q + 1)
                            nc.vector.tensor_tensor_scan(st[k][:, :], dA[k], dBu[k], 0.0, ALU.mult, ALU.add).then_inc(scanned, 1)
                            dve.wait_ge(scanned, q + 1)
                            dve.wait_ge(c_full, q + 1)
                            wait(dve, prod_used, q - 1)
                            nc.vector.tensor_tensor(prod[k], st[k][:, :], c_ps[:, :], ALU.mult).then_inc(prod_ready, 1)
                        step(0, 0)
                        step(1, 1)
                        with dve.Fori(0, (NS - 2) // 2) as i:
                            step(i * 2 + 2, 0)
                            step(i * 2 + 3, 1)
                        dve.wait_ge(prod_used, s * ALLN + h * NS + NS)
                        nc.vector.scalar_tensor_tensor(out=y[:, h, :], in0=u[slot][:, h, :], scalar=d_skip[:, h:h + 1],
                                                       in1=y_ps[:, :], op0=ALU.mult, op1=ALU.add).then_inc(y_ready, 1)
                for g in range(2):
                    use = Use(back_use, s, g)
                    use.read(dve)
                    t = s * 2 + g
                    nc.vector.tensor_tensor(c.x[:, at(t, GRP), :], c.x[:, at(t, GRP), :],
                                            use.ps[:, :].rearrange("p (j d) -> p j d", j=GRP), ALU.add).then_inc(use.free, 1)
            order(dve, front, rest_of)


def store_result(nc, c, out):
    with ExitStack() as ctx:
        stored = nc.alloc_semaphore("stored")
        block = ctx.enter_context(nc.Block())
        o_v = out.rearrange("b s d -> (b s) d").rearrange("(j p) d -> p j d", p=P)

        @block.sync
        def _(sp):
            for q in range(4):
                sp.dma_start(o_v[:, at(q, NT // 4), :], c.x[:, at(q, NT // 4), :]).then_inc(stored, 16)
            sp.wait_ge(stored, 64)


def program(nc, a, out, stages=range(6)):
    with ExitStack() as ctx:
        def sb(name, shape, dt=F32):
            return ctx.enter_context(nc.sbuf_tensor(name, shape, dt))
        c = Core()
        c.x = sb("x_res", [P, NT, D])
        c.ident = sb("ident", [P, P])
        c.before = sb("before", [P, P], BF16)
        c.ones_bf = sb("ones_bf", [P, P], BF16)
        c.ones_f = sb("ones_f", [P, NT])
        c.minus_half = sb("minus_half", [P, NT])
        c.expert_id = sb("expert_id", [P, NT, E])
        c.drop_row = sb("drop_row", [P, 1])
        c.block_row = sb("block_row", [P, NBLK + 2])
        c.rows_in = nc.dram_tensor("rows_in", [ROWS + P, D], F32, kind="Internal").ap()
        c.rows_out = nc.dram_tensor("rows_out", [ROWS, D], F32, kind="Internal").ap()
        load_and_constants(nc, c, a["L0_attn_x"])

        def moe0(tag):
            w = {"gate": a["L0_ffn_Wg"], "gate_b": a["L0_ffn_bg"], "ln_w": a["L0_ffn_ln_w"],
                 "packed": [(a["L0_ffn_W1a"].rearrange("e d f -> d e f"), 0, F),
                            (a["L0_ffn_W1b"].rearrange("e d f -> d e f"), F, F)]
                 + [(a["L0_ffn_W2"][:, at(k, P), :].rearrange("e f d -> f e d"), 2 * F + k * D, D) for k in range(FC)],
                 "b1a": a["L0_ffn_b1a"], "b1b": a["L0_ffn_b1b"], "b2": a["L0_ffn_b2"],
                 "n_loads": 2 + FC + 2 * FC + 1}
            moe(nc, c, tag, True, w)

        def moe1(tag):
            w = {"gate": a["L1_ffn_router_w"].rearrange("e d -> d e"),
                 "packed": [(a["L1_ffn_w1"].rearrange("e d f -> d e f"), 0, F)]
                 + [(a["L1_ffn_w2"][:, at(k, P), :].rearrange("e f d -> f e d"), F + k * D, D) for k in range(FC)],
                 "n_loads": 1 + FC}
            moe(nc, c, tag, False, w)

        def scan0(tag):
            scan_layer(nc, c, tag, False, {
                "w_in": a["L0_attn_W_in"], "w_out": a["L0_attn_W_out"], "conv_w": a["L0_attn_conv_w"],
                "d_skip": a["L0_attn_D_param"], "dt_b": a["L0_attn_b_dt"], "w_x": a["L0_attn_W_x"],
                "w_dt": a["L0_attn_W_dt"], "w_b": a["L0_attn_W_Bp"]})

        def scan1(tag):
            scan_layer(nc, c, tag, True, {
                "w_in": a["in_proj_T"], "w_out": a["out_proj_T"], "conv_w": a["L1_attn_conv_w"],
                "conv_b": a["L1_attn_conv_b"], "d_skip": a["L1_attn_Dskip"], "dt_b": a["L1_attn_dt_proj_b"],
                "a_log": a["L1_attn_A_log"], "w_x": a["x_proj_T"], "w_dt": a["dt_proj_T"]})

        steps = [lambda: moe0("m0"), lambda: scan0("s0"), lambda: moe0("m1"),
                 lambda: moe1("m2"), lambda: scan1("s1"), lambda: moe1("m3")]
        for s in stages:
            with layer_semaphores(nc):
                steps[s]()
        store_result(nc, c, out)


def laid_out(inputs):
    a = {k: np.ascontiguousarray(v) for k, v in inputs.items()}
    a["in_proj_T"] = np.ascontiguousarray(a["L1_attn_in_proj_w"].T)
    a["out_proj_T"] = np.ascontiguousarray(a["L1_attn_out_proj_w"].T)
    a["x_proj_T"] = np.ascontiguousarray(a["L1_attn_x_proj_w"].reshape(4, 48, 64).transpose(2, 0, 1))
    a["dt_proj_T"] = np.ascontiguousarray(a["L1_attn_dt_proj_w"].reshape(4, 64, 16).transpose(2, 0, 1))
    for name in ("L1_attn_in_proj_w", "L1_attn_out_proj_w", "L1_attn_x_proj_w", "L1_attn_dt_proj_w"):
        del a[name]
    return a


def kernel(**inputs):
    import concourse.bacc as bacc
    from concourse.bass_utils import run_bass_kernel_spmd

    nc = bacc.Bacc("TRN2", target_bir_lowering=False, num_devices=1)
    arrays = laid_out(inputs)
    aps = {k: nc.dram_tensor(f"in_{k}", v.shape, mybir.dt.from_np(v.dtype), kind="ExternalInput").ap()
           for k, v in arrays.items()}
    out = nc.dram_tensor("out_x", (SEQS, SEQ, D), F32, kind="ExternalOutput").ap()
    program(nc, aps, out)
    r = run_bass_kernel_spmd(nc, [{f"in_{k}": v for k, v in arrays.items()}], core_ids=[0])
    return r.results[0]["out_x"]
```
